# Optimizing a Trainium2 kernel written in Bass

```python
import numpy as np
import jax
import jax.numpy as jnp

def _softmax(x, axis=-1):
    return jax.nn.softmax(x, axis=axis)

def _gelu(x):
    return jax.nn.gelu(x, approximate=True)

def _silu(x):
    return jax.nn.silu(x)

def _sigmoid(x):
    return jax.nn.sigmoid(x)

def _layernorm(x, axis=-1, eps=1e-05):
    m = jnp.mean(x, axis=axis, keepdims=True)
    v = jnp.var(x, axis=axis, keepdims=True)
    return (x - m) / jnp.sqrt(v + eps)

def _scatter_add(tgt, idx, src, axis=0):
    return tgt.at[idx].add(src)

def _segment_sum(src, seg, n):
    return jax.ops.segment_sum(src, seg, n)
kernel_name = 'mk_adj_preln_d1_adj_r2_04ade3'

def setup_inputs(seed: int=0):
    np.random.seed(seed)
    _w = jnp.asarray

    def _rec_inputs():
        import jax
        import jax.numpy as jnp
        _gk = jax.random.key(seed)
        x = -0.0002928 + 1 * jax.random.normal(jax.random.fold_in(_gk, 1), (4096, 256), jnp.float32)
        _w = (1.0 + jnp.arange(4096, dtype=jnp.float32)) ** (-0.5)
        _w = _w / _w.mean()
        _pij = jnp.clip(0.000488281 * _w[:, None] * _w[None, :], 0.0, 1.0)
        _a = jax.random.uniform(jax.random.fold_in(_gk, 2), (4096, 4096)) < _pij
        _a = jnp.logical_or(_a, jnp.eye(4096, dtype=bool))
        _af = _a.astype(jnp.float32)
        _af = _af * jax.random.uniform(jax.random.fold_in(_gk, 3), (4096, 4096), jnp.float32, 0.05, 1)
        adj = _af
        return (x, adj)
    x, adj = _rec_inputs()

    def _L0_gnn_setup():
        import jax, jax.numpy as jnp
        import numpy as np
        N = 4096
        D = 256
        key = jax.random.key(seed)
        k_h, k_a, k_q, k_k, k_v = jax.random.split(key, 5)
        H = jax.random.normal(k_h, (N, D), dtype=jnp.float32)
        A = jax.random.uniform(k_a, (N, N), dtype=jnp.float32)
        W_Q = jax.random.uniform(k_q, (D, D), dtype=jnp.float32)
        W_K = jax.random.uniform(k_k, (D, D), dtype=jnp.float32)
        W_V = jax.random.uniform(k_v, (D, D), dtype=jnp.float32)
        return {'H': H, 'A': A, 'W_Q': W_Q, 'W_K': W_K, 'W_V': W_V}
    _L0_gnn_all = _L0_gnn_setup()
    _L0_gnn_in = {k: v for k, v in _L0_gnn_all.items() if k in ('W_Q', 'W_K', 'W_V')}
    del _L0_gnn_all
    return {'x': x, 'adj': adj, 'L0_gnn_W_Q': _L0_gnn_in['W_Q'], 'L0_gnn_W_K': _L0_gnn_in['W_K'], 'L0_gnn_W_V': _L0_gnn_in['W_V']}

def reference(x, adj, L0_gnn_W_Q, L0_gnn_W_K, L0_gnn_W_V):
    import jax
    import jax.numpy as jnp

    def _L0_gnn_ref(H, A, W_Q, W_K, W_V):
        import jax, jax.numpy as jnp
        import numpy as np
        N = 4096
        D = 256
        scale = 1.0 / jnp.sqrt(jnp.asarray(H.shape[1], dtype=H.dtype))
        HQ = H @ W_Q
        HK = H @ W_K
        scores = jnp.einsum('nd,md->nm', HQ, HK)
        scores = scores * A * scale
        attn = jax.nn.softmax(scores, axis=1)
        return attn @ (H @ W_V)
    h = jnp.maximum(_layernorm(x, axis=-1), 0.0)
    x = x + _L0_gnn_ref(h, adj, L0_gnn_W_Q, L0_gnn_W_K, L0_gnn_W_V)
    return x

_drawn_inputs = setup_inputs


def setup_inputs(seed=0):
    import zlib

    import numpy as np

    out = dict(_drawn_inputs(seed))
    spreads = {}
    factors = {}
    for name, (base, spread) in spreads.items():
        noise = np.random.default_rng([zlib.crc32(name.encode()), seed]).standard_normal(out[name].shape)
        drawn = base * np.exp(spread * noise) if base else spread * noise
        out[name] = jnp.asarray(drawn.astype(out[name].dtype))
    for name, factor in factors.items():
        out[name] = (out[name] * factor).astype(out[name].dtype)
    return out
```

```python
from contextlib import ExitStack

import concourse.bass as bass
from concourse import mybir

F32 = mybir.dt.float32
F16 = mybir.dt.float16
U32 = mybir.dt.uint32
ALU = mybir.AluOpType
ACT = mybir.ActivationFunctionType
AX_X = mybir.AxisListType.X
ABSMAX = bass.bass_isa.ReduceOp.absmax

P = 128
BANK = 512
LN_EPS = 1e-5
LOWEST = -3.4e38
TINY = 1e-30
EXPONENT_BITS = 0x7F800000

H_UP = 16.0
W_TOP = 16.0


def gnn_layer(nc, x, adj, w_q, w_k, w_v, out):
    N, D = x.shape
    DC = D // P
    TILES = N // P
    CH = N // BANK
    PAIRS = CH // 2
    BPC = BANK // P
    GROUPS = TILES // BPC
    ABUFS = 4
    UNROLL = 4
    assert CH == 8 and DC == 2 and TILES % UNROLL == 0

    RING_PER_TILE = CH + 1
    RING_HEAD = 4

    adj_v = adj.rearrange("(t p) m -> t p m", p=P)
    x_tiles = x.rearrange("(t p) d -> t p d", p=P)
    out_tiles = out.rearrange("(t p) d -> t p d", p=P)
    x_groups = x.rearrange("(g b p) d -> g p b d", p=P, b=BPC)

    ctx = ExitStack()
    with ctx:
        def sb(name, shape, dt=F32):
            return ctx.enter_context(nc.sbuf_tensor(name, shape, dt))

        def sem(name):
            return ctx.enter_context(nc.semaphore(name))

        ident = sb("ident", [P, P])
        ln_eps = sb("ln_eps", [P, 1])
        w_in = sb("w_in", [P, 3, DC, D])
        wq_t = sb("wq_t", [P, DC, D])
        wk_t = sb("wk_t", [P, DC, D])
        m_raw = sb("m_raw", [P, DC, D])
        w_max = sb("w_max", [P, 2])
        w_gmax = sb("w_gmax", [P, 2])
        w_pow = sb("w_pow", [P, 2])
        w_inv = sb("w_inv", [P, 2])
        w_up = sb("w_up", [P, 2])
        exp_scale = sb("exp_scale", [P, 1])
        neg_exp_scale = sb("neg_exp_scale", [P, 1])
        v_scale = sb("v_scale", [P, 1])
        m_hi = sb("m_hi", [P, DC, D], F16)
        m_lo = sb("m_lo", [P, DC, D], F16)
        wv_hi = sb("wv_hi", [P, DC, D], F16)
        wv_lo = sb("wv_lo", [P, DC, D], F16)

        x_grp = sb("x_grp", [P, 2, BPC, D])
        bn = sb("bn", [P, 2, BPC, 6])
        mean_var = sb("mean_var", [P, 2, BPC, 2])
        std = sb("std", [P, 2, BPC, 1])
        rstd = sb("rstd", [P, 2, BPC, 1])

        ht_hi = sb("ht_hi", [P, DC, N], F16)
        ht_lo = sb("ht_lo", [P, DC, N], F16)
        v_hl = sb("v_hl", [P, TILES, 2 * D], F16)
        g_hi = sb("g_hi", [P, 2, DC, P], F16)
        g_lo = sb("g_lo", [P, 2, DC, P], F16)

        prob = sb("prob", [P, ABUFS, N])
        p_max = sb("p_max", [P, 2, PAIRS])
        exp_bias = sb("exp_bias", [P, 2])
        p_sum = sb("p_sum", [P, 2, PAIRS])
        p_tot = sb("p_tot", [P, 2])
        p_inv = sb("p_inv", [P, 2])
        o_scale = sb("o_scale", [P, 2])
        pt_hi = sb("pt_hi", [P, 4, BANK], F16)
        pt_lo = sb("pt_lo", [P, 4, BANK], F16)
        x_out = sb("x_out", [P, 2, D])

        ps_s = ctx.enter_context(nc.psum_tensor("ps_s", [P, 2, 2 * BANK], F32))
        ps_ring = ctx.enter_context(nc.psum_tensor("ps_ring", [P, 2, BANK], F32))
        ps_o = ctx.enter_context(nc.psum_tensor("ps_o", [P, 2, BANK], F32))

        w_loaded = sem("w_loaded")
        x_loaded = [sem(f"x_loaded{b}") for b in range(2)]
        adj_loaded = [sem(f"adj_loaded{b}") for b in range(ABUFS)]
        res_loaded = [sem(f"res_loaded{b}") for b in range(2)]
        stored = sem("stored")
        ident_zero = sem("ident_zero")
        ident_ready = sem("ident_ready")
        eps_ready = sem("eps_ready")
        w_transposed = sem("w_transposed")
        wq_t_ready = sem("wq_t_ready")
        wk_t_ready = sem("wk_t_ready")
        m_product = sem("m_product")
        m_raw_ready = sem("m_raw_ready")
        w_max_ready = sem("w_max_ready")
        w_gmax_ready = sem("w_gmax_ready")
        w_chain = sem("w_chain")
        w_up_ready = sem("w_up_ready")
        w_hi_ready = sem("w_hi_ready")
        w_lo_ready = sem("w_lo_ready")
        bn_done = sem("bn_done")
        var_ready = sem("var_ready")
        std_ready = sem("std_ready")
        rstd_ready = sem("rstd_ready")
        norm_ready = sem("norm_ready")
        ht_full = sem("ht_full")
        ht_hi_done = sem("ht_hi_done")
        ht_lo_done = sem("ht_lo_done")
        v_full = sem("v_full")
        v_hi_done = sem("v_hi_done")
        v_lo_done = sem("v_lo_done")
        score_full = sem("score_full")
        scaled = sem("scaled")
        bias_ready = sem("bias_ready")
        exp_done = sem("exp_done")
        ring_full = sem("ring_full")
        ring_hi = sem("ring_hi")
        ring_lo = sem("ring_lo")
        o_full = sem("o_full")
        o_chain = sem("o_chain")
        out_ready = sem("out_ready")
        waited = sem("waited")

        block = ctx.enter_context(nc.Block())

        def lin(i, per, k):
            return i * per + k

        def main_turns(eng, body):
            with eng.Fori(0, TILES // UNROLL - 1) as i:
                for j in range(UNROLL):
                    body(i, j, False)
            for j in range(UNROLL):
                body(TILES // UNROLL - 1, j, True)

        T_ITEM = [7 - RING_PER_TILE, 8 - RING_PER_TILE, 0, 1, 3, 4, 5, 6]
        G_ITEM = 2 - 2 * RING_PER_TILE

        def absent(i, j, k):
            if not isinstance(i, int) or i < TILES // UNROLL - 1:
                return 0
            return max(0, j - (UNROLL - 2) + (k >= 2))

        def ring_count(i, j, k):
            return lin(i, UNROLL * RING_PER_TILE, RING_HEAD + j * RING_PER_TILE + k + 1 - absent(i, j, k))

        def ring_bank(i, j, k):
            return (RING_HEAD + j * RING_PER_TILE + k - absent(i, j, k)) % 2

        @block.sync
        def _(sp):
            for n, w in enumerate((w_q, w_k, w_v)):
                sp.dma_start(w_in[:, n, :, :], w.rearrange("(c p) n -> p c n", p=P)).then_inc(w_loaded, 16)
                if n == 0:
                    sp.dma_start(x_grp[:, 0], x_groups[0]).then_inc(x_loaded[0], 16)
            sp.dma_start(x_grp[:, 1], x_groups[1]).then_inc(x_loaded[1], 16)
            with sp.Fori(0, GROUPS // 2 - 1) as i:
                for c in range(2):
                    sp.wait_ge(ht_full, lin(i, 2, c + 1))
                    src = x.rearrange("(i c b p) d -> i c p b d", c=2, b=BPC, p=P)[1:]
                    sp.dma_start(x_grp[:, c], src[bass.ds(i, 1), c].rearrange("i p b d -> (i p) b d")
                                 ).then_inc(x_loaded[c], 16)
            for t in range(ABUFS):
                sp.dma_start(prob[:, t, :], adj_v[t]).then_inc(adj_loaded[t], 16)
                if t < 2:
                    sp.dma_start(x_out[:, t, :], x_tiles[t]).then_inc(res_loaded[t], 16)

            def tile_turn(i, j, last):
                t = UNROLL * i + j
                if not last:
                    sp.wait_ge(ring_full, ring_count(i, j, T_ITEM[7]))
                    sp.dma_start(prob[:, j, :], adj[bass.ds((t + ABUFS) * P, P), :]
                                 ).then_inc(adj_loaded[j], 16)
                sp.wait_ge(out_ready, lin(i, UNROLL, j + 1))
                sp.dma_start(out[bass.ds(t * P, P), :], x_out[:, j % 2, :]).then_inc(stored, 16)
                sp.wait_ge(stored, lin(i, 16 * UNROLL, 16 * (j + 1)))
                if not last or j < UNROLL - 2:
                    sp.dma_start(x_out[:, j % 2, :], x[bass.ds((t + 2) * P, P), :]
                                 ).then_inc(res_loaded[j % 2], 16)

            main_turns(sp, tile_turn)

        @block.gpsimd
        def _(pool):
            nc.gpsimd.memset(ident[:], 0.0).then_inc(ident_zero, 1)
            pool.wait_ge(ident_zero, 1)
            nc.gpsimd.affine_select(out=ident[:], in_=ident[:], compare_op=ALU.not_equal, fill=1.0, base=0,
                                    pattern=[[-1, P]], channel_multiplier=1).then_inc(ident_ready, 1)
            nc.gpsimd.memset(ln_eps[:], LN_EPS / H_UP ** 2).then_inc(eps_ready, 1)
            pool.wait_ge(w_max_ready, 2)
            nc.gpsimd.partition_all_reduce(w_gmax[:, :], w_max[:, :], P, ABSMAX).then_inc(w_gmax_ready, 1)

        @block.tensor
        def _(pe):
            pe.wait_ge(w_loaded, 48)
            pe.wait_ge(ident_ready, 1)
            for n in range(2):
                for k in range(DC):
                    for c in range(DC):
                        last = nc.tensor.transpose(ps_o[:, n, k * D + c * P:k * D + (c + 1) * P],
                                                   w_in[:, n, c, k * P:(k + 1) * P], ident[:])
            last.then_inc(w_transposed, 1)
            pe.wait_ge(wq_t_ready, 1)
            pe.wait_ge(wk_t_ready, 1)
            for c in range(DC):
                for k in range(DC):
                    last = nc.tensor.matmul(ps_ring[:, 0, c * D:(c + 1) * D], wq_t[:, k, c * P:(c + 1) * P],
                                            wk_t[:, k, :], start=(k == 0), stop=(k == DC - 1))
            last.then_inc(m_product, 1)

            def transpose_h(i, c):
                pe.wait_ge(norm_ready, lin(i, 2, c + 1))
                if c >= 2:
                    pe.wait_ge(ht_lo_done, lin(i, 2, c - 1))
                for d in range(DC):
                    for b in range(BPC):
                        last = nc.tensor.transpose(ps_s[:, c % 2, d * BANK + b * P:d * BANK + (b + 1) * P],
                                                   x_grp[:, c % 2, b, d * P:(d + 1) * P], ident[:])
                last.then_inc(ht_full, 1)

            def project_v(i, c):
                pe.wait_ge(ht_lo_done, lin(i, 2, c + 1))
                bank = ps_ring if c % 2 == 0 else ps_o
                for b in range(BPC):
                    dst = bank[:, b // 2, (b % 2) * D:(b % 2 + 1) * D]
                    row = lin(i, 2 * BANK, c * BANK + b * P)
                    for d in range(DC):
                        for n, (h, w) in enumerate(((ht_hi, wv_hi), (ht_hi, wv_lo), (ht_lo, wv_hi))):
                            last = nc.tensor.matmul(dst, h[:, d, bass.ds(row, P)], w[:, d, :],
                                                    start=(d == 0 and n == 0), stop=(d == DC - 1 and n == 2))
                last.then_inc(v_full, 1)

            transpose_h(0, 0)
            pe.wait_ge(w_lo_ready, 2)
            transpose_h(0, 1)
            project_v(0, 0)
            with pe.Fori(0, GROUPS // 2 - 1) as i:
                for c in (2, 3):
                    transpose_h(i, c)
                    project_v(i, c - 1)
            pe.wait_ge(v_lo_done, GROUPS - 2)
            project_v(GROUPS // 2 - 1, 1)

            def g_tile(u, i, j, k):
                bank = ps_ring[:, ring_bank(i, j, k), :]
                for e in range(DC):
                    for d in range(DC):
                        for n, (m, h) in enumerate(((m_hi, ht_hi), (m_hi, ht_lo), (m_lo, ht_hi))):
                            last = nc.tensor.matmul(bank[:, e * P:(e + 1) * P], m[:, d, e * P:(e + 1) * P],
                                                    h[:, d, bass.ds(u * P, P)],
                                                    start=(d == 0 and n == 0), stop=(d == DC - 1 and n == 2))
                last.then_inc(ring_full, 1)

            def score_chunk(i, j, s):
                if s % 2 == 0:
                    if not (isinstance(i, int) and UNROLL * i + j == 0 and s < 4):
                        pe.wait_ge(scaled, lin(i, UNROLL * PAIRS, PAIRS * j + s // 2 - 1))
                if s == 0:
                    if isinstance(i, int) and UNROLL * i + j < 2:
                        pe.wait_ge(ring_lo, UNROLL * i + j + 1)
                    else:
                        pe.wait_ge(ring_lo, ring_count(i, j, G_ITEM))
                b = j % 2
                dst = ps_s[:, (s // 2) % 2, (s % 2) * BANK:(s % 2 + 1) * BANK]
                cols = slice(s * BANK, (s + 1) * BANK)
                for d in range(DC):
                    for n, (g, h) in enumerate(((g_hi, ht_hi), (g_hi, ht_lo), (g_lo, ht_hi))):
                        last = nc.tensor.matmul(dst, g[:, b, d, :], h[:, d, cols],
                                                start=(d == 0 and n == 0), stop=(d == DC - 1 and n == 2))
                if s % 2 == 1:
                    last.then_inc(score_full, 1)

            def transpose_chunk(i, j, s):
                k = T_ITEM[s]
                if s % 2 == 0:
                    pe.wait_ge(exp_done, lin(i, UNROLL * PAIRS, PAIRS * j + s // 2 + 1))
                pe.wait_ge(ring_lo, ring_count(i, j, k) - 2)
                for b in range(BPC):
                    col = s * BANK + b * P
                    last = nc.tensor.transpose(ps_ring[:, ring_bank(i, j, k), b * P:(b + 1) * P],
                                               prob[:, j % ABUFS, col:col + P], ident[:])
                last.then_inc(ring_full, 1)

            def weigh_values(i, j, s):
                pe.wait_ge(ring_lo, ring_count(i, j, T_ITEM[s]))
                for b in range(BPC):
                    m = s * BPC + b
                    nc.tensor.matmul(ps_o[:, j % 2, :], pt_hi[:, s % 4, b * P:(b + 1) * P], v_hl[:, m, :],
                                     start=(m == 0), stop=False)
                    last = nc.tensor.matmul(ps_o[:, j % 2, 0:D], pt_lo[:, s % 4, b * P:(b + 1) * P],
                                            v_hl[:, m, 0:D], start=False, stop=(m == TILES - 1))
                if s == CH - 1:
                    last.then_inc(o_full, 1)

            pe.wait_ge(v_lo_done, GROUPS - 1)
            g_tile(0, 0, 0, -4)
            g_tile(1, 0, 0, -3)
            for s in range(CH):
                score_chunk(0, 0, s)
            pe.wait_ge(v_lo_done, GROUPS)
            for s in range(3):
                score_chunk(0, 1, s)
                if s > 0:
                    transpose_chunk(0, 0, s - 1)

            def tile_turn(i, j, last):
                def after(n):
                    return i, j + n
                more = [not last or j + n < UNROLL for n in range(3)]
                for r in range(CH):
                    if r < CH - 3:
                        if more[1]:
                            score_chunk(*after(1), r + 3)
                        transpose_chunk(i, j, r + 2)
                    else:
                        if more[2]:
                            score_chunk(*after(2), r - 5)
                        if r == CH - 3:
                            transpose_chunk(i, j, CH - 1)
                        elif more[1]:
                            transpose_chunk(*after(1), r - 6)
                    if r == 1 and more[2]:
                        pe.wait_ge(ring_lo, ring_count(i, j, 0))
                        g_tile(UNROLL * i + j + 2, i, j, 2)
                    weigh_values(i, j, r)

            main_turns(pe, tile_turn)

        @block.scalar
        def _(act):
            act.wait_ge(w_transposed, 1)
            nc.scalar.copy(wq_t[:].rearrange("p a b -> p (a b)"), ps_o[:, 0, :]).then_inc(wq_t_ready, 1)
            act.wait_ge(m_product, 1)
            nc.scalar.copy(m_raw[:].rearrange("p a b -> p (a b)"), ps_ring[:, 0, :]).then_inc(m_raw_ready, 1)

            def std_of(i, c):
                act.wait_ge(var_ready, lin(i, 2, c + 1))
                nc.scalar.activation(std[:, c % 2], mean_var[:, c % 2, :, 1:2], ACT.Sqrt, bias=ln_eps[:, 0:1],
                                     scale=1.0 / H_UP ** 2).then_inc(std_ready, 1)

            def h_high(i, c):
                act.wait_ge(ht_full, lin(i, 2, c + 1))
                nc.scalar.activation(ht_hi[:, :, bass.ds(lin(i, 2 * BANK, c * BANK), BANK)],
                                     ps_s[:, c % 2, :].rearrange("p (d n) -> p d n", d=DC),
                                     ACT.Relu).then_inc(ht_hi_done, 1)

            def v_high(i, c):
                act.wait_ge(v_full, lin(i, 2, c + 1))
                bank = ps_ring if c % 2 == 0 else ps_o
                nc.scalar.copy(v_hl[:, bass.ds(lin(i, 2 * BPC, c * BPC), BPC), 0:D],
                               bank[:, :, :].rearrange("p a (b d) -> p (a b) d", d=D)).then_inc(v_hi_done, 1)

            act.wait_ge(eps_ready, 1)
            std_of(0, 0)
            act.wait_ge(w_up_ready, 1)
            nc.scalar.mul(m_hi[:], m_raw[:], w_up[:, 0:1]).then_inc(w_hi_ready, 1)
            nc.scalar.mul(wv_hi[:], w_in[:, 2], w_up[:, 1:2]).then_inc(w_hi_ready, 1)
            h_high(0, 0)
            std_of(0, 1)
            h_high(0, 1)
            v_high(0, 0)
            with act.Fori(0, GROUPS // 2 - 1) as i:
                for c in (2, 3):
                    std_of(i, c)
                    h_high(i, c)
                    v_high(i, c - 1)
            v_high(GROUPS // 2 - 1, 1)

            def ring_high(i, j, k, dst):
                act.wait_ge(ring_full, ring_count(i, j, k))
                width = BANK if dst.shape[-1] == BANK else DC * P
                src = ps_ring[:, ring_bank(i, j, k), 0:width]
                if width != BANK:
                    src = src.rearrange("p (e n) -> p e n", e=DC)
                nc.scalar.copy(dst, src).then_inc(ring_hi, 1)

            def bias_of(i, j):
                act.wait_ge(scaled, lin(i, UNROLL * PAIRS, PAIRS * (j + 1)))
                nc.scalar.mul(exp_bias[:, j % 2:j % 2 + 1], p_max[:, j % 2, PAIRS - 1:PAIRS],
                              neg_exp_scale[:, 0:1]).then_inc(bias_ready, 1)
                act.wait_ge(bias_ready, lin(i, UNROLL, j + 1))

            def exp_pair(i, j, q):
                v = prob[:, j % ABUFS, q * 2 * BANK:(q + 1) * 2 * BANK]
                nc.scalar.activation(v, v, ACT.Exp, bias=exp_bias[:, j % 2:j % 2 + 1], scale=exp_scale[:, 0:1],
                                     accum_out=p_sum[:, j % 2, q:q + 1]).then_inc(exp_done, 1)

            ring_high(0, 0, -4, g_hi[:, 0])
            ring_high(0, 0, -3, g_hi[:, 1])
            bias_of(0, 0)
            exp_pair(0, 0, 0)
            exp_pair(0, 0, 1)
            ring_high(0, 0, -2, pt_hi[:, 0, :])
            ring_high(0, 0, -1, pt_hi[:, 1, :])

            def tile_turn(i, j, last):
                def after(n):
                    return i, j + n
                more = [not last or j + n < UNROLL for n in range(3)]
                ring_high(i, j, T_ITEM[2], pt_hi[:, 2, :])
                exp_pair(i, j, 2)
                ring_high(i, j, T_ITEM[3], pt_hi[:, 3, :])
                if more[2]:
                    ring_high(i, j, 2, g_hi[:, j % 2])
                ring_high(i, j, T_ITEM[4], pt_hi[:, 0, :])
                exp_pair(i, j, 3)
                for s in range(5, CH):
                    ring_high(i, j, T_ITEM[s], pt_hi[:, s % 4, :])
                if more[1]:
                    bias_of(*after(1))
                    exp_pair(*after(1), 0)
                    ring_high(*after(1), T_ITEM[0], pt_hi[:, 0, :])
                    exp_pair(*after(1), 1)
                    ring_high(*after(1), T_ITEM[1], pt_hi[:, 1, :])

            main_turns(act, tile_turn)

        @block.vector
        def _(dve):
            dve.wait_ge(w_loaded, 48)
            nc.vector.tensor_reduce(w_max[:, 1:2], w_in[:, 2], mybir.AxisListType.XY, ALU.max, apply_absolute_value=True
                                    ).then_inc(w_max_ready, 1)
            dve.wait_ge(w_transposed, 1)
            nc.vector.tensor_copy(wk_t[:].rearrange("p a b -> p (a b)"), ps_o[:, 1, :]).then_inc(wk_t_ready, 1)

            def stand_alone():
                dve.sem_inc(waited, 1)

            def stats(i, c):
                dve.wait_ge(x_loaded[c % 2], lin(i, 16, 16 * (c // 2 + 1)))
                for b in range(BPC):
                    nc.vector.bn_stats(bn[:, c % 2, b, :], x_grp[:, c % 2, b, :]).then_inc(bn_done, 1)
                dve.wait_ge(bn_done, lin(i, 2 * BPC, (c + 1) * BPC))
                stand_alone()
                for b in range(BPC):
                    last = nc.vector.bn_aggr(mean_var[:, c % 2, b, :], bn[:, c % 2, b, :])
                last.then_inc(var_ready, 1)

            def normalise(i, c):
                dve.wait_ge(std_ready, lin(i, 2, c + 1))
                nc.vector.reciprocal(rstd[:, c % 2], std[:, c % 2]).then_inc(rstd_ready, 1)
                dve.wait_ge(rstd_ready, lin(i, 2, c + 1))
                for b in range(BPC):
                    v = x_grp[:, c % 2, b, :]
                    last = nc.vector.tensor_scalar(v, v, mean_var[:, c % 2, b, 0:1], rstd[:, c % 2, b, :],
                                                   ALU.subtract, ALU.mult)
                last.then_inc(norm_ready, 1)

            def h_low(i, c):
                dve.wait_ge(ht_hi_done, lin(i, 2, c + 1))
                cols = bass.ds(lin(i, 2 * BANK, c * BANK), BANK)
                nc.vector.scalar_tensor_tensor(out=ht_lo[:, :, cols],
                                               in0=ps_s[:, c % 2, :].rearrange("p (d n) -> p d n", d=DC),
                                               scalar=0.0, in1=ht_hi[:, :, cols], op0=ALU.max,
                                               op1=ALU.subtract).then_inc(ht_lo_done, 1)

            def v_low(i, c):
                dve.wait_ge(v_hi_done, lin(i, 2, c + 1))
                bank = ps_ring if c % 2 == 0 else ps_o
                tiles = bass.ds(lin(i, 2 * BPC, c * BPC), BPC)
                nc.vector.tensor_tensor(v_hl[:, tiles, D:2 * D],
                                        bank[:, :, :].rearrange("p a (b d) -> p (a b) d", d=D),
                                        v_hl[:, tiles, 0:D], ALU.subtract).then_inc(v_lo_done, 1)

            stats(0, 0)
            dve.wait_ge(m_product, 1)
            dve.wait_ge(m_raw_ready, 1)
            nc.vector.tensor_reduce(w_max[:, 0:1], m_raw[:], mybir.AxisListType.XY, ALU.max, apply_absolute_value=True
                                    ).then_inc(w_max_ready, 1)
            normalise(0, 0)
            stats(0, 1)

            dve.wait_ge(w_gmax_ready, 1)
            nc.vector.tensor_scalar_max(w_inv[:], w_gmax[:], TINY).then_inc(w_chain, 1)
            dve.wait_ge(w_chain, 1)
            nc.vector.tensor_scalar(w_pow[:].bitcast(U32), w_inv[:].bitcast(U32), EXPONENT_BITS, None,
                                    ALU.bitwise_and).then_inc(w_chain, 1)
            dve.wait_ge(w_chain, 2)
            nc.vector.reciprocal(w_inv[:], w_pow[:]).then_inc(w_chain, 1)
            nc.vector.tensor_scalar(exp_scale[:], w_pow[:, 0:1], 2 / W_TOP / H_UP ** 2 / D ** 0.5, None, ALU.mult)
            nc.vector.tensor_scalar(neg_exp_scale[:], w_pow[:, 0:1], -2 / W_TOP / H_UP ** 2 / D ** 0.5, None,
                                    ALU.mult)
            nc.vector.tensor_scalar(v_scale[:], w_pow[:, 1:2], 2 / W_TOP / H_UP, None,
                                    ALU.mult).then_inc(w_chain, 1)
            dve.wait_ge(w_chain, 4)
            nc.vector.tensor_scalar(w_up[:], w_inv[:], W_TOP / 2, None, ALU.mult).then_inc(w_up_ready, 1)
            dve.wait_ge(w_up_ready, 1)
            for n, (raw, hi, lo) in enumerate(((m_raw[:], m_hi, m_lo), (w_in[:, 2], wv_hi, wv_lo))):
                dve.wait_ge(w_hi_ready, n + 1)
                nc.vector.scalar_tensor_tensor(out=lo[:], in0=raw, scalar=w_up[:, n:n + 1], in1=hi[:],
                                               op0=ALU.mult, op1=ALU.subtract).then_inc(w_lo_ready, 1)
            h_low(0, 0)
            normalise(0, 1)
            with dve.Fori(0, GROUPS // 2 - 1) as i:
                for c in (1, 2):
                    stats(i, c + 1)
                    h_low(i, c)
                    v_low(i, c - 1)
                    normalise(i, c + 1)
            h_low(GROUPS // 2 - 1, 1)
            v_low(GROUPS // 2 - 1, 0)
            v_low(GROUPS // 2 - 1, 1)

            def ring_low(i, j, k, hi, dst):
                dve.wait_ge(ring_hi, ring_count(i, j, k))
                width = BANK if dst.shape[-1] == BANK else DC * P
                src = ps_ring[:, ring_bank(i, j, k), 0:width]
                if width != BANK:
                    src = src.rearrange("p (e n) -> p e n", e=DC)
                nc.vector.tensor_tensor(dst, src, hi, ALU.subtract).then_inc(ring_lo, 1)

            def scale_pair(i, j, q):
                if q == 0:
                    dve.wait_ge(adj_loaded[j % ABUFS], lin(i, 16, 16 * (j // ABUFS + 1)))
                    start = LOWEST
                else:
                    dve.wait_ge(scaled, lin(i, UNROLL * PAIRS, PAIRS * j + q))
                    start = p_max[:, j % 2, q - 1:q]
                dve.wait_ge(score_full, lin(i, UNROLL * PAIRS, PAIRS * j + q + 1))
                stand_alone()
                v = prob[:, j % ABUFS, q * 2 * BANK:(q + 1) * 2 * BANK]
                nc.vector.tensor_tensor_reduce(out=v, in0=ps_s[:, q % 2, :], in1=v, scale=1.0, scalar=start,
                                               op0=ALU.mult, op1=ALU.max,
                                               accum_out=p_max[:, j % 2, q:q + 1]).then_inc(scaled, 1)

            def result(i, j):
                b = j % 2
                dve.wait_ge(exp_done, lin(i, UNROLL * PAIRS, PAIRS * (j + 1)))
                nc.vector.reduce_sum(p_tot[:, b:b + 1], p_sum[:, b, :], AX_X).then_inc(o_chain, 1)
                dve.wait_ge(o_chain, lin(i, 4 * UNROLL, 4 * j + 1))
                nc.vector.reciprocal(p_inv[:, b:b + 1], p_tot[:, b:b + 1]).then_inc(o_chain, 1)
                dve.wait_ge(o_chain, lin(i, 4 * UNROLL, 4 * j + 2))
                nc.vector.tensor_tensor(o_scale[:, b:b + 1], p_inv[:, b:b + 1], v_scale[:],
                                        ALU.mult).then_inc(o_chain, 1)
                dve.wait_ge(o_chain, lin(i, 4 * UNROLL, 4 * j + 3))
                dve.wait_ge(o_full, lin(i, UNROLL, j + 1))
                dve.wait_ge(res_loaded[b], lin(i, 16 * UNROLL // 2, 16 * (j // 2 + 1)))
                nc.vector.scalar_tensor_tensor(out=x_out[:, b, :], in0=ps_o[:, b, D:2 * D],
                                               scalar=o_scale[:, b:b + 1], in1=x_out[:, b, :], op0=ALU.mult,
                                               op1=ALU.add).then_inc(o_chain, 1)
                dve.wait_ge(o_chain, lin(i, 4 * UNROLL, 4 * j + 4))
                nc.vector.scalar_tensor_tensor(out=x_out[:, b, :], in0=ps_o[:, b, 0:D],
                                               scalar=o_scale[:, b:b + 1], in1=x_out[:, b, :], op0=ALU.mult,
                                               op1=ALU.add).then_inc(out_ready, 1)

            ring_low(0, 0, -4, g_hi[:, 0], g_lo[:, 0])
            ring_low(0, 0, -3, g_hi[:, 1], g_lo[:, 1])
            for q in range(PAIRS):
                scale_pair(0, 0, q)
            ring_low(0, 0, -2, pt_hi[:, 0, :], pt_lo[:, 0, :])
            scale_pair(0, 1, 0)
            ring_low(0, 0, -1, pt_hi[:, 1, :], pt_lo[:, 1, :])

            def tile_turn(i, j, last):
                def after(n):
                    return i, j + n
                more = [not last or j + n < UNROLL for n in range(3)]

                def low(at, s):
                    ring_low(*at, T_ITEM[s], pt_hi[:, s % 4, :], pt_lo[:, s % 4, :])

                for r in range(CH - 3):
                    if r % 2 == 0 and more[1]:
                        scale_pair(*after(1), r // 2 + 1)
                    low((i, j), r + 2)
                    if r == 1 and more[2]:
                        ring_low(i, j, 2, g_hi[:, j % 2], g_lo[:, j % 2])
                low((i, j), CH - 1)
                if more[1]:
                    if more[2]:
                        scale_pair(*after(2), 0)
                    low(after(1), 0)
                    low(after(1), 1)
                result(i, j)

            main_turns(dve, tile_turn)


_INS = ["x", "adj", "L0_gnn_W_Q", "L0_gnn_W_K", "L0_gnn_W_V"]
_OUTS = [((4096, 256), "float32")]


def kernel(**inputs):
    import numpy as _np
    import concourse.bacc as _bacc
    from concourse import mybir as _mybir
    from concourse.bass_utils import run_bass_kernel_spmd as _run

    nc = _bacc.Bacc("TRN2", target_bir_lowering=False, num_devices=1)
    arrays, args = {}, []
    for name in _INS:
        a = _np.ascontiguousarray(inputs[name])
        arrays[f"in_{name}_dram"] = a
        args.append(nc.dram_tensor(f"in_{name}_dram", a.shape, _mybir.dt.from_np(a.dtype), kind="ExternalInput").ap())
    for i, (shape, dtype) in enumerate(_OUTS):
        dt = _mybir.dt.from_np(_np.dtype(dtype))
        args.append(nc.dram_tensor(f"out_{i}_dram", shape, dt, kind="ExternalOutput").ap())
    gnn_layer(nc, *args)
    r = _run(nc, [arrays], core_ids=[0])
    got = tuple(r.results[0][f"out_{i}_dram"] for i in range(len(_OUTS)))
    return got[0]
```

```python
from contextlib import ExitStack

import concourse.bass as bass
from concourse import mybir

F32 = mybir.dt.float32
F16 = mybir.dt.float16
U32 = mybir.dt.uint32
ALU = mybir.AluOpType
ACT = mybir.ActivationFunctionType
AX_X = mybir.AxisListType.X
AX_XY = mybir.AxisListType.XY
ABSMAX = bass.bass_isa.ReduceOp.absmax

P = 128
BANK = 512
LN_EPS = 1e-5
LOWEST = -3.4e38
TINY = 1e-30
EXPONENT_BITS = 0x7F800000

H_UP = 16.0
W_TOP = 16.0


def gnn_layer(nc, x, adj, w_q, w_k, w_v, out):
    N, D = x.shape
    DC = D // P
    TILES = N // P
    CH = N // BANK
    PAIRS = CH // 2
    PAIR = 2 * BANK
    BPP = PAIR // P
    BPC = BANK // P
    GROUPS = TILES // BPC
    ABUFS = 4
    UNROLL = 4
    LEAD = 6
    G_STEP = 3
    assert CH == 8 and DC == 2 and TILES % UNROLL == 0 and GROUPS == CH

    x_tiles = x.rearrange("(t p) d -> t p d", p=P)
    adj_tiles = adj.rearrange("(t p) m -> t p m", p=P)
    x_groups = x.rearrange("(g b p) d -> g p b d", p=P, b=BPC)

    ctx = ExitStack()
    with ctx:
        def sb(name, shape, dt=F32):
            return ctx.enter_context(nc.sbuf_tensor(name, shape, dt))

        def sem(name):
            return ctx.enter_context(nc.semaphore(name))

        ident = sb("ident", [P, P])
        ln_eps = sb("ln_eps", [P, 1])
        w_in = sb("w_in", [P, 3, DC, D])
        wq_t = sb("wq_t", [P, DC, D])
        wk_t = sb("wk_t", [P, DC, D])
        m_raw = sb("m_raw", [P, DC, D])
        w_max = sb("w_max", [P, 2])
        w_gmax = sb("w_gmax", [P, 2])
        w_pow = sb("w_pow", [P, 2])
        w_inv = sb("w_inv", [P, 2])
        w_up = sb("w_up", [P, 2])
        exp_scale = sb("exp_scale", [P, 1])
        neg_exp_scale = sb("neg_exp_scale", [P, 1])
        v_scale = sb("v_scale", [P, 1])
        m_hi = sb("m_hi", [P, DC, D], F16)
        m_lo = sb("m_lo", [P, DC, D], F16)
        wv_hi = sb("wv_hi", [P, DC, D], F16)
        wv_lo = sb("wv_lo", [P, DC, D], F16)

        bn = sb("bn", [P, TILES, 6])
        mean_var = sb("mean_var", [P, TILES, 2])
        std = sb("std", [P, TILES, 1])
        rstd = sb("rstd", [P, TILES, 1])

        ht_hi = sb("ht_hi", [P, DC, N], F16)
        ht_lo = sb("ht_lo", [P, DC, N], F16)
        v_hl = sb("v_hl", [P, TILES, 2 * D], F16)
        g_hi = sb("g_hi", [P, 2, DC, P], F16)
        g_lo = sb("g_lo", [P, 2, DC, P], F16)

        prob = sb("prob", [P, ABUFS, N])
        p_max = sb("p_max", [P, 2, PAIRS])
        exp_bias = sb("exp_bias", [P, 2])
        p_sum = sb("p_sum", [P, 2, PAIRS])
        p_tot = sb("p_tot", [P, 2])
        p_inv = sb("p_inv", [P, 2])
        o_scale = sb("o_scale", [P, 2])
        parts = sb("parts", [P, 2, 2, PAIR], F16)
        parts_t = sb("parts_t", [P, PAIRS, 2, BPP, P], F16)
        x_out = sb("x_out", [P, 2, D])

        x_rows = prob[:, 2:4, :].rearrange("p a (g b d) -> p (a g) b d", b=BPC, d=D)

        ps_s = ctx.enter_context(nc.psum_tensor("ps_s", [P, 2, PAIR], F32))
        ps_g = ctx.enter_context(nc.psum_tensor("ps_g", [P, 2, BANK], F32))
        ps_o = ctx.enter_context(nc.psum_tensor("ps_o", [P, 2, BANK], F32))

        w_loaded = sem("w_loaded")
        x_loaded = [sem(f"x_loaded{g}") for g in range(GROUPS)]
        adj_loaded = [sem(f"adj_loaded{b}") for b in range(ABUFS)]
        res_loaded = [sem(f"res_loaded{b}") for b in range(2)]
        stored = sem("stored")
        ident_zero = sem("ident_zero")
        ident_ready = sem("ident_ready")
        eps_ready = sem("eps_ready")
        w_transposed = sem("w_transposed")
        wq_t_ready = sem("wq_t_ready")
        wk_t_ready = sem("wk_t_ready")
        m_product = sem("m_product")
        m_raw_ready = sem("m_raw_ready")
        w_max_ready = sem("w_max_ready")
        w_gmax_ready = sem("w_gmax_ready")
        w_chain = sem("w_chain")
        w_up_ready = sem("w_up_ready")
        w_hi_ready = sem("w_hi_ready")
        w_lo_ready = sem("w_lo_ready")
        bn_done = sem("bn_done")
        var_ready = sem("var_ready")
        std_ready = sem("std_ready")
        rstd_ready = sem("rstd_ready")
        norm_ready = sem("norm_ready")
        ht_full = sem("ht_full")
        ht_hi_done = sem("ht_hi_done")
        ht_lo_done = sem("ht_lo_done")
        v_full = sem("v_full")
        v_hi_done = sem("v_hi_done")
        v_lo_done = sem("v_lo_done")
        g_full = sem("g_full")
        g_hi_done = sem("g_hi_done")
        g_lo_done = sem("g_lo_done")
        score_full = sem("score_full")
        scaled = sem("scaled")
        bias_ready = sem("bias_ready")
        exp_done = sem("exp_done")
        high_done = sem("high_done")
        low_done = sem("low_done")
        turned = [sem(f"turned{b}") for b in range(2)]
        weighed = sem("weighed")
        o_chain = sem("o_chain")
        out_ready = sem("out_ready")
        waited_dve = sem("waited_dve")
        waited_sp = sem("waited_sp")

        block = ctx.enter_context(nc.Block())

        def lin(i, per, k):
            return i * per + k

        def main_turns(eng, body):
            with eng.Fori(0, TILES // UNROLL - 1) as i:
                for j in range(UNROLL):
                    body(i, j, False)
            for j in range(UNROLL):
                body(TILES // UNROLL - 1, j, True)

        def there(j, last):
            return not last or j < UNROLL

        @block.sync
        def _(sp):
            sp.dma_start(x_rows[:, 0], x_groups[0]).then_inc(x_loaded[0], 16)
            for n, w in enumerate((w_q, w_k, w_v)):
                sp.dma_start(w_in[:, n, :, :], w.rearrange("(c p) n -> p c n", p=P)).then_inc(w_loaded, 16)
            for g in range(1, GROUPS):
                sp.dma_start(x_rows[:, g], x_groups[g]).then_inc(x_loaded[g], 16)
                if g == 2:
                    sp.dma_start(prob[:, 0, :], adj_tiles[0]).then_inc(adj_loaded[0], 16)
            sp.dma_start(prob[:, 1, :], adj_tiles[1]).then_inc(adj_loaded[1], 16)
            for t in range(2):
                sp.dma_start(x_out[:, t, :], x_tiles[t]).then_inc(res_loaded[t], 16)
            for b in (2, 3):
                sp.wait_ge(ht_full, (b - 1) * GROUPS // 2)
                sp.dma_start(prob[:, b, :], adj_tiles[b]).then_inc(adj_loaded[b], 16)

            def await_count(semaphore, count):
                sp.wait_ge(semaphore, count)
                if not isinstance(count, int):
                    sp.sem_inc(waited_sp, 1)

            def transpose_pair(i, j, q):
                await_count(low_done, lin(i, UNROLL * PAIRS, PAIRS * j + q + 1))
                if not (isinstance(i, int) and UNROLL * i + j == 0):
                    await_count(weighed, lin(i, UNROLL * PAIRS, PAIRS * (j - 1) + q + 1))
                sp.dma_start_transpose(parts_t[:, q].rearrange("p h b n -> p (h b) n"),
                                       parts[:, q % 2].rearrange("p h m -> p (h m)")).then_inc(turned[q % 2], 16)

            def load_adj(i, j):
                row = (UNROLL * i + j) * P
                sp.dma_start(prob[:, j % ABUFS, :], adj[bass.ds(row, P), :]).then_inc(adj_loaded[j % ABUFS], 16)

            for q in range(PAIRS):
                transpose_pair(0, 0, q)

            def tile_turn(i, j, last):
                if not last:
                    load_adj(i, j + ABUFS)
                if there(j + 1, last):
                    for q in range(PAIRS):
                        transpose_pair(i, j + 1, q)
                t = UNROLL * i + j
                await_count(out_ready, lin(i, UNROLL, j + 1))
                sp.dma_start(out[bass.ds(t * P, P), :], x_out[:, j % 2, :]).then_inc(stored, 16)
                await_count(stored, lin(i, 16 * UNROLL, 16 * (j + 1)))
                if there(j + 2, last):
                    sp.dma_start(x_out[:, j % 2, :], x[bass.ds((t + 2) * P, P), :]
                                 ).then_inc(res_loaded[j % 2], 16)

            main_turns(sp, tile_turn)

        @block.gpsimd
        def _(pool):
            nc.gpsimd.memset(ln_eps[:], LN_EPS / H_UP ** 2).then_inc(eps_ready, 1)
            nc.gpsimd.memset(ident[:], 0.0).then_inc(ident_zero, 1)
            pool.wait_ge(ident_zero, 1)
            nc.gpsimd.affine_select(out=ident[:], in_=ident[:], compare_op=ALU.not_equal, fill=1.0, base=0,
                                    pattern=[[-1, P]], channel_multiplier=1).then_inc(ident_ready, 1)

            def normalise(g):
                pool.wait_ge(rstd_ready, g + 1)
                for b in range(BPC):
                    t = g * BPC + b
                    last = nc.gpsimd.tensor_scalar(x_rows[:, g, b, :], x_rows[:, g, b, :], mean_var[:, t, 0:1],
                                                   rstd[:, t, :], ALU.subtract, ALU.mult)
                last.then_inc(norm_ready, 1)

            normalise(0)
            pool.wait_ge(w_max_ready, 2)
            nc.gpsimd.partition_all_reduce(w_gmax[:, :], w_max[:, :], P, ABSMAX).then_inc(w_gmax_ready, 1)
            for g in range(1, GROUPS):
                normalise(g)

        @block.tensor
        def _(pe):
            pe.wait_ge(w_loaded, 48)
            pe.wait_ge(ident_ready, 1)
            for n in range(2):
                for k in range(DC):
                    for c in range(DC):
                        last = nc.tensor.transpose(ps_o[:, n, k * D + c * P:k * D + (c + 1) * P],
                                                   w_in[:, n, c, k * P:(k + 1) * P], ident[:])
            last.then_inc(w_transposed, 1)
            pe.wait_ge(wq_t_ready, 1)
            pe.wait_ge(wk_t_ready, 1)
            for c in range(DC):
                for k in range(DC):
                    last = nc.tensor.matmul(ps_s[:, 0, c * D:(c + 1) * D], wq_t[:, k, c * P:(c + 1) * P],
                                            wk_t[:, k, :], start=(k == 0), stop=(k == DC - 1))
            last.then_inc(m_product, 1)

            def transpose_h(g):
                pe.wait_ge(norm_ready, g + 1)
                if g > 0:
                    pe.wait_ge(ht_lo_done, g)
                for d in range(DC):
                    for b in range(BPC):
                        last = nc.tensor.transpose(ps_g[:, d, b * P:(b + 1) * P],
                                                   x_rows[:, g, b, d * P:(d + 1) * P], ident[:])
                last.then_inc(ht_full, 1)

            def project_v(g):
                pe.wait_ge(ht_lo_done, g + 1)
                if g > 0:
                    pe.wait_ge(v_lo_done, g)
                for b in range(BPC):
                    dst = ps_o[:, b // 2, (b % 2) * D:(b % 2 + 1) * D]
                    rows = slice((g * BPC + b) * P, (g * BPC + b + 1) * P)
                    for d in range(DC):
                        for n, (h, w) in enumerate(((ht_hi, wv_hi), (ht_hi, wv_lo), (ht_lo, wv_hi))):
                            last = nc.tensor.matmul(dst, h[:, d, rows], w[:, d, :],
                                                    start=(d == 0 and n == 0), stop=(d == DC - 1 and n == 2))
                last.then_inc(v_full, 1)

            def g_tile(i, j, bank):
                col = (UNROLL * i + j) * P
                for e in range(DC):
                    for d in range(DC):
                        for n, (m, h) in enumerate(((m_hi, ht_hi), (m_hi, ht_lo), (m_lo, ht_hi))):
                            last = nc.tensor.matmul(bank[:, e * P:(e + 1) * P], m[:, d, e * P:(e + 1) * P],
                                                    h[:, d, bass.ds(col, P)],
                                                    start=(d == 0 and n == 0), stop=(d == DC - 1 and n == 2))
                last.then_inc(g_full, 1)

            def score_chunk(i, j, s):
                if s % 2 == 0 and not (isinstance(i, int) and UNROLL * i + j == 0 and s < 4):
                    pe.wait_ge(scaled, lin(i, UNROLL * PAIRS, PAIRS * j + s // 2 - 1))
                if s == 0:
                    pe.wait_ge(g_lo_done, lin(i, UNROLL, j + 1))
                b = j % 2
                dst = ps_s[:, (s // 2) % 2, (s % 2) * BANK:(s % 2 + 1) * BANK]
                cols = slice(s * BANK, (s + 1) * BANK)
                for d in range(DC):
                    for n, (g, h) in enumerate(((g_hi, ht_hi), (g_hi, ht_lo), (g_lo, ht_hi))):
                        last = nc.tensor.matmul(dst, g[:, b, d, :], h[:, d, cols],
                                                start=(d == 0 and n == 0), stop=(d == DC - 1 and n == 2))
                if s % 2 == 1:
                    last.then_inc(score_full, 1)

            def weigh_values(i, j, s):
                q = s // 2
                if s % 2 == 0:
                    pe.wait_ge(turned[q % 2], lin(i, 32 * UNROLL, 32 * j + 16 * (q // 2 + 1)))
                for b in range(BPC):
                    m = s * BPC + b
                    col = (s % 2) * BPC + b
                    nc.tensor.matmul(ps_o[:, j % 2, :], parts_t[:, q, 0, col, :], v_hl[:, m, :],
                                     start=(m == 0), stop=False)
                    last = nc.tensor.matmul(ps_o[:, j % 2, 0:D], parts_t[:, q, 1, col, :],
                                            v_hl[:, m, 0:D], start=False, stop=(m == TILES - 1))
                if s % 2 == 1:
                    last.then_inc(weighed, 1)

            transpose_h(0)
            pe.wait_ge(w_lo_ready, 2)
            pe.wait_ge(ht_lo_done, 1)
            g_tile(0, 0, ps_s[:, 1, :])
            for g in range(GROUPS):
                if g + 1 < GROUPS:
                    transpose_h(g + 1)
                pe.wait_ge(ht_lo_done, g + 1)
                score_chunk(0, 0, g)
                if g == GROUPS - 1:
                    g_tile(0, 1, ps_g[:, 1, :])
                    g_tile(0, 2, ps_g[:, 0, :])
                project_v(g)
            for s in range(LEAD):
                score_chunk(0, 1, s)
            pe.wait_ge(v_lo_done, GROUPS)

            def tile_turn(i, j, last):
                for r in range(CH):
                    if r < CH - LEAD:
                        if there(j + 1, last):
                            score_chunk(i, j + 1, r + LEAD)
                    elif there(j + 2, last):
                        score_chunk(i, j + 2, r + LEAD - CH)
                    if r == G_STEP and there(j + 3, last):
                        g_tile(i, j + 3, ps_g[:, (j + 3) % 2, :])
                    weigh_values(i, j, r)

            main_turns(pe, tile_turn)

        @block.scalar
        def _(act):
            def std_of(g):
                act.wait_ge(var_ready, g + 1)
                tiles = slice(g * BPC, (g + 1) * BPC)
                nc.scalar.activation(std[:, tiles], mean_var[:, tiles, 1:2], ACT.Sqrt, bias=ln_eps[:, 0:1],
                                     scale=1.0 / H_UP ** 2).then_inc(std_ready, 1)

            def h_high(g):
                act.wait_ge(ht_full, g + 1)
                nc.scalar.activation(ht_hi[:, :, g * BANK:(g + 1) * BANK], ps_g[:, :, :],
                                     ACT.Relu).then_inc(ht_hi_done, 1)

            def v_high(g):
                act.wait_ge(v_full, g + 1)
                nc.scalar.copy(v_hl[:, g * BPC:(g + 1) * BPC, 0:D],
                               ps_o[:, :, :].rearrange("p a (b d) -> p (a b) d", d=D)).then_inc(v_hi_done, 1)

            def g_high(i, j, bank):
                act.wait_ge(g_full, lin(i, UNROLL, j + 1))
                nc.scalar.copy(g_hi[:, j % 2], bank[:, 0:D].rearrange("p (e n) -> p e n", e=DC)
                               ).then_inc(g_hi_done, 1)

            act.wait_ge(eps_ready, 1)
            std_of(0)
            act.wait_ge(w_transposed, 1)
            nc.scalar.copy(wq_t[:].rearrange("p a b -> p (a b)"), ps_o[:, 0, :]).then_inc(wq_t_ready, 1)
            act.wait_ge(m_product, 1)
            nc.scalar.copy(m_raw[:].rearrange("p a b -> p (a b)"), ps_s[:, 0, 0:2 * D]).then_inc(m_raw_ready, 1)
            h_high(0)
            std_of(1)
            act.wait_ge(w_up_ready, 1)
            nc.scalar.mul(m_hi[:], m_raw[:], w_up[:, 0:1]).then_inc(w_hi_ready, 1)
            nc.scalar.mul(wv_hi[:], w_in[:, 2], w_up[:, 1:2]).then_inc(w_hi_ready, 1)
            g_high(0, 0, ps_s[:, 1, :])
            std_of(2)
            for g in range(GROUPS):
                if g + 1 < GROUPS:
                    h_high(g + 1)
                if g + 3 < GROUPS:
                    std_of(g + 3)
                if g == GROUPS - 1:
                    g_high(0, 1, ps_g[:, 1, :])
                    g_high(0, 2, ps_g[:, 0, :])
                v_high(g)

            def bias_of(i, j):
                act.wait_ge(scaled, lin(i, UNROLL * PAIRS, PAIRS * (j + 1)))
                nc.scalar.mul(exp_bias[:, j % 2:j % 2 + 1], p_max[:, j % 2, PAIRS - 1:PAIRS],
                              neg_exp_scale[:, 0:1]).then_inc(bias_ready, 1)
                act.wait_ge(bias_ready, lin(i, UNROLL, j + 1))

            def exp_pair(i, j, q):
                v = prob[:, j % ABUFS, q * PAIR:(q + 1) * PAIR]
                nc.scalar.activation(v, v, ACT.Exp, bias=exp_bias[:, j % 2:j % 2 + 1], scale=exp_scale[:, 0:1],
                                     accum_out=p_sum[:, j % 2, q:q + 1]).then_inc(exp_done, 1)

            def high_parts(i, j, q):
                if not (isinstance(i, int) and UNROLL * i + j == 0 and q < 2):
                    act.wait_ge(turned[q % 2], lin(i, 32 * UNROLL, 32 * j + 16 * (q // 2)))
                act.wait_ge(exp_done, lin(i, UNROLL * PAIRS, PAIRS * j + q + 1))
                nc.scalar.copy(parts[:, q % 2, 0, :], prob[:, j % ABUFS, q * PAIR:(q + 1) * PAIR]
                               ).then_inc(high_done, 1)

            def exponentials(i, j, between):
                bias_of(i, j)
                for q in range(PAIRS):
                    exp_pair(i, j, q)
                    high_parts(i, j, q)
                    if q == 1:
                        between()

            exponentials(0, 0, lambda: None)

            def tile_turn(i, j, last):
                def g_next():
                    if there(j + 3, last):
                        g_high(i, j + 3, ps_g[:, (j + 3) % 2, :])
                if there(j + 1, last):
                    exponentials(i, j + 1, g_next)

            main_turns(act, tile_turn)

        @block.vector
        def _(dve):
            def stats(g):
                dve.wait_ge(x_loaded[g], 16)
                for b in range(BPC):
                    nc.vector.bn_stats(bn[:, g * BPC + b, :], x_rows[:, g, b, :]).then_inc(bn_done, 1)
                for b in range(BPC):
                    t = g * BPC + b
                    dve.wait_ge(bn_done, t + 1)
                    last = nc.vector.bn_aggr(mean_var[:, t, :], bn[:, t, :])
                last.then_inc(var_ready, 1)

            def rstd_of(g):
                dve.wait_ge(std_ready, g + 1)
                tiles = slice(g * BPC, (g + 1) * BPC)
                nc.vector.reciprocal(rstd[:, tiles], std[:, tiles]).then_inc(rstd_ready, 1)

            def h_low(g):
                dve.wait_ge(ht_hi_done, g + 1)
                cols = slice(g * BANK, (g + 1) * BANK)
                nc.vector.scalar_tensor_tensor(out=ht_lo[:, :, cols], in0=ps_g[:, :, :], scalar=0.0,
                                               in1=ht_hi[:, :, cols], op0=ALU.max,
                                               op1=ALU.subtract).then_inc(ht_lo_done, 1)

            def v_low(g):
                dve.wait_ge(v_hi_done, g + 1)
                tiles = slice(g * BPC, (g + 1) * BPC)
                nc.vector.tensor_tensor(v_hl[:, tiles, D:2 * D],
                                        ps_o[:, :, :].rearrange("p a (b d) -> p (a b) d", d=D),
                                        v_hl[:, tiles, 0:D], ALU.subtract).then_inc(v_lo_done, 1)

            def g_low(i, j, bank):
                dve.wait_ge(g_hi_done, lin(i, UNROLL, j + 1))
                nc.vector.tensor_tensor(g_lo[:, j % 2], bank[:, 0:D].rearrange("p (e n) -> p e n", e=DC),
                                        g_hi[:, j % 2], ALU.subtract).then_inc(g_lo_done, 1)

            def stand_alone():
                dve.sem_inc(waited_dve, 1)

            def scale_pair(i, j, q):
                if q == 0:
                    dve.wait_ge(adj_loaded[j % ABUFS], lin(i, 16, 16 * (j // ABUFS + 1)))
                    start = LOWEST
                else:
                    dve.wait_ge(scaled, lin(i, UNROLL * PAIRS, PAIRS * j + q))
                    start = p_max[:, j % 2, q - 1:q]
                dve.wait_ge(score_full, lin(i, UNROLL * PAIRS, PAIRS * j + q + 1))
                if not isinstance(i, int):
                    stand_alone()
                v = prob[:, j % ABUFS, q * PAIR:(q + 1) * PAIR]
                nc.vector.tensor_tensor_reduce(out=v, in0=ps_s[:, q % 2, :], in1=v, scale=1.0, scalar=start,
                                               op0=ALU.mult, op1=ALU.max,
                                               accum_out=p_max[:, j % 2, q:q + 1]).then_inc(scaled, 1)

            def low_parts(i, j, q):
                dve.wait_ge(high_done, lin(i, UNROLL * PAIRS, PAIRS * j + q + 1))
                nc.vector.tensor_tensor(parts[:, q % 2, 1, :], prob[:, j % ABUFS, q * PAIR:(q + 1) * PAIR],
                                        parts[:, q % 2, 0, :], ALU.subtract).then_inc(low_done, 1)

            stats(0)
            rstd_of(0)
            dve.wait_ge(w_loaded, 48)
            nc.vector.tensor_reduce(w_max[:, 1:2], w_in[:, 2], AX_XY, ALU.max, apply_absolute_value=True
                                    ).then_inc(w_max_ready, 1)
            dve.wait_ge(w_transposed, 1)
            nc.vector.tensor_copy(wk_t[:].rearrange("p a b -> p (a b)"), ps_o[:, 1, :]).then_inc(wk_t_ready, 1)
            stats(1)
            dve.wait_ge(m_raw_ready, 1)
            nc.vector.tensor_reduce(w_max[:, 0:1], m_raw[:], AX_XY, ALU.max, apply_absolute_value=True
                                    ).then_inc(w_max_ready, 1)
            h_low(0)
            rstd_of(1)

            dve.wait_ge(w_gmax_ready, 1)
            nc.vector.tensor_scalar_max(w_inv[:], w_gmax[:], TINY).then_inc(w_chain, 1)
            dve.wait_ge(w_chain, 1)
            nc.vector.tensor_scalar(w_pow[:].bitcast(U32), w_inv[:].bitcast(U32), EXPONENT_BITS, None,
                                    ALU.bitwise_and).then_inc(w_chain, 1)
            dve.wait_ge(w_chain, 2)
            nc.vector.reciprocal(w_inv[:], w_pow[:]).then_inc(w_chain, 1)
            dve.wait_ge(w_chain, 3)
            nc.vector.tensor_scalar(w_up[:], w_inv[:], W_TOP / 2, None, ALU.mult).then_inc(w_up_ready, 1)
            nc.vector.tensor_scalar(exp_scale[:], w_pow[:, 0:1], 2 / W_TOP / H_UP ** 2 / D ** 0.5, None, ALU.mult)
            nc.vector.tensor_scalar(neg_exp_scale[:], w_pow[:, 0:1], -2 / W_TOP / H_UP ** 2 / D ** 0.5, None,
                                    ALU.mult)
            nc.vector.tensor_scalar(v_scale[:], w_pow[:, 1:2], 2 / W_TOP / H_UP, None, ALU.mult)
            dve.wait_ge(w_up_ready, 1)
            for n, (raw, hi, lo) in enumerate(((m_raw[:], m_hi, m_lo), (w_in[:, 2], wv_hi, wv_lo))):
                dve.wait_ge(w_hi_ready, n + 1)
                nc.vector.scalar_tensor_tensor(out=lo[:], in0=raw, scalar=w_up[:, n:n + 1], in1=hi[:],
                                               op0=ALU.mult, op1=ALU.subtract).then_inc(w_lo_ready, 1)
            g_low(0, 0, ps_s[:, 1, :])
            stats(2)
            for g in range(GROUPS):
                if g + 1 < GROUPS:
                    h_low(g + 1)
                if g + 2 < GROUPS:
                    rstd_of(g + 2)
                if g + 3 < GROUPS:
                    stats(g + 3)
                if g % 2 == 1:
                    scale_pair(0, 0, g // 2)
                if g == GROUPS - 1:
                    g_low(0, 1, ps_g[:, 1, :])
                    g_low(0, 2, ps_g[:, 0, :])
                v_low(g)

            def result(i, j):
                b = j % 2
                dve.wait_ge(exp_done, lin(i, UNROLL * PAIRS, PAIRS * (j + 1)))
                nc.vector.reduce_sum(p_tot[:, b:b + 1], p_sum[:, b, :], AX_X).then_inc(o_chain, 1)
                dve.wait_ge(o_chain, lin(i, 4 * UNROLL, 4 * j + 1))
                nc.vector.reciprocal(p_inv[:, b:b + 1], p_tot[:, b:b + 1]).then_inc(o_chain, 1)
                dve.wait_ge(o_chain, lin(i, 4 * UNROLL, 4 * j + 2))
                nc.vector.tensor_tensor(o_scale[:, b:b + 1], p_inv[:, b:b + 1], v_scale[:],
                                        ALU.mult).then_inc(o_chain, 1)
                dve.wait_ge(o_chain, lin(i, 4 * UNROLL, 4 * j + 3))
                dve.wait_ge(weighed, lin(i, UNROLL * PAIRS, PAIRS * (j + 1)))
                dve.wait_ge(res_loaded[b], lin(i, 16 * UNROLL // 2, 16 * (j // 2 + 1)))
                nc.vector.scalar_tensor_tensor(out=x_out[:, b, :], in0=ps_o[:, b, D:2 * D],
                                               scalar=o_scale[:, b:b + 1], in1=x_out[:, b, :], op0=ALU.mult,
                                               op1=ALU.add).then_inc(o_chain, 1)
                dve.wait_ge(o_chain, lin(i, 4 * UNROLL, 4 * j + 4))
                nc.vector.scalar_tensor_tensor(out=x_out[:, b, :], in0=ps_o[:, b, 0:D],
                                               scalar=o_scale[:, b:b + 1], in1=x_out[:, b, :], op0=ALU.mult,
                                               op1=ALU.add).then_inc(out_ready, 1)

            low_parts(0, 0, 0)
            scale_pair(0, 1, 0)
            low_parts(0, 0, 1)
            low_parts(0, 0, 2)
            scale_pair(0, 1, 1)
            low_parts(0, 0, 3)
            scale_pair(0, 1, 2)

            def tile_turn(i, j, last):
                if there(j + 1, last):
                    scale_pair(i, j + 1, 3)
                    low_parts(i, j + 1, 0)
                    if there(j + 2, last):
                        scale_pair(i, j + 2, 0)
                    low_parts(i, j + 1, 1)
                    if there(j + 3, last):
                        g_low(i, j + 3, ps_g[:, (j + 3) % 2, :])
                    low_parts(i, j + 1, 2)
                    low_parts(i, j + 1, 3)
                    if there(j + 2, last):
                        scale_pair(i, j + 2, 1)
                        scale_pair(i, j + 2, 2)
                result(i, j)

            main_turns(dve, tile_turn)


_INS = ["x", "adj", "L0_gnn_W_Q", "L0_gnn_W_K", "L0_gnn_W_V"]
_OUTS = [((4096, 256), "float32")]


def kernel(**inputs):
    import numpy as _np
    import concourse.bacc as _bacc
    from concourse import mybir as _mybir
    from concourse.bass_utils import run_bass_kernel_spmd as _run

    nc = _bacc.Bacc("TRN2", target_bir_lowering=False, num_devices=1)
    arrays, args = {}, []
    for name in _INS:
        a = _np.ascontiguousarray(inputs[name])
        arrays[f"in_{name}_dram"] = a
        args.append(nc.dram_tensor(f"in_{name}_dram", a.shape, _mybir.dt.from_np(a.dtype), kind="ExternalInput").ap())
    for i, (shape, dtype) in enumerate(_OUTS):
        dt = _mybir.dt.from_np(_np.dtype(dtype))
        args.append(nc.dram_tensor(f"out_{i}_dram", shape, dt, kind="ExternalOutput").ap())
    gnn_layer(nc, *args)
    r = _run(nc, [arrays], core_ids=[0])
    got = tuple(r.results[0][f"out_{i}_dram"] for i in range(len(_OUTS)))
    return got[0]
```

```python
from contextlib import ExitStack

import concourse.bass as bass
from concourse import mybir

F32 = mybir.dt.float32
F16 = mybir.dt.float16
U32 = mybir.dt.uint32
ALU = mybir.AluOpType
ACT = mybir.ActivationFunctionType
AX_X = mybir.AxisListType.X
AX_XY = mybir.AxisListType.XY
ABSMAX = bass.bass_isa.ReduceOp.absmax

P = 128
BANK = 512
LN_EPS = 1e-5
LOWEST = -3.4e38
TINY = 1e-30
EXPONENT_BITS = 0x7F800000

H_UP = 16.0
W_TOP = 16.0


def gnn_layer(nc, x, adj, w_q, w_k, w_v, out):
    N, D = x.shape
    DC = D // P
    TILES = N // P
    CH = N // BANK
    PAIRS = CH // 2
    PAIR = 2 * BANK
    BPP = PAIR // P
    BPC = BANK // P
    GROUPS = TILES // BPC
    ABUFS = 4
    UNROLL = 4
    LEAD = 6
    LATE_V = 2
    G_STEP = 3
    assert CH == 8 and DC == 2 and TILES % UNROLL == 0 and GROUPS == CH

    x_tiles = x.rearrange("(t p) d -> t p d", p=P)
    adj_tiles = adj.rearrange("(t p) m -> t p m", p=P)
    x_groups = x.rearrange("(g b p) d -> g p b d", p=P, b=BPC)

    ctx = ExitStack()
    with ctx:
        def sb(name, shape, dt=F32):
            return ctx.enter_context(nc.sbuf_tensor(name, shape, dt))

        def sem(name):
            return ctx.enter_context(nc.semaphore(name))

        ident = sb("ident", [P, P])
        ln_eps = sb("ln_eps", [P, 1])
        w_in = sb("w_in", [P, 3, DC, D])
        wq_t = sb("wq_t", [P, DC, D])
        wk_t = sb("wk_t", [P, DC, D])
        m_raw = sb("m_raw", [P, DC, D])
        w_max = sb("w_max", [P, 2])
        w_gmax = sb("w_gmax", [P, 2])
        w_floor = sb("w_floor", [P, 2])
        w_pow = sb("w_pow", [P, 2])
        w_inv = sb("w_inv", [P, 2])
        w_up = sb("w_up", [P, 2])
        exp_scale = sb("exp_scale", [P, 1])
        neg_exp_scale = sb("neg_exp_scale", [P, 1])
        v_scale = sb("v_scale", [P, 1])
        m_hi = sb("m_hi", [P, DC, D], F16)
        m_lo = sb("m_lo", [P, DC, D], F16)
        wv_hi = sb("wv_hi", [P, DC, D], F16)
        wv_lo = sb("wv_lo", [P, DC, D], F16)

        bn = sb("bn", [P, TILES, 6])
        mean_var = sb("mean_var", [P, TILES, 2])
        std = sb("std", [P, TILES, 1])
        rstd = sb("rstd", [P, TILES, 1])
        neg_mean = sb("neg_mean", [P, TILES, 1])
        table_warm = sb("table_warm", [P, 2])

        ht_hi = sb("ht_hi", [P, DC, N], F16)
        ht_lo = sb("ht_lo", [P, DC, N], F16)
        v_hl = sb("v_hl", [P, TILES, 2 * D], F16)
        g_hi = sb("g_hi", [P, 2, DC, P], F16)
        g_lo = sb("g_lo", [P, 2, DC, P], F16)

        prob = sb("prob", [P, ABUFS, N])
        p_max = sb("p_max", [P, 2, PAIRS])
        exp_bias = sb("exp_bias", [P, 2])
        p_sum = sb("p_sum", [P, 2, PAIRS])
        p_tot = sb("p_tot", [P, 2])
        p_inv = sb("p_inv", [P, 2])
        o_scale = sb("o_scale", [P, 2])
        parts = sb("parts", [P, PAIRS, 2, PAIR], F16)
        parts_t = sb("parts_t", [P, PAIRS, 2, BPP, P], F16)
        x_out = sb("x_out", [P, 2, D])

        x_rows = prob[:, 2:4, :].rearrange("p a (g b d) -> p (a g) b d", b=BPC, d=D)

        ps_s = ctx.enter_context(nc.psum_tensor("ps_s", [P, 2, PAIR], F32))
        ps_g = ctx.enter_context(nc.psum_tensor("ps_g", [P, 2, BANK], F32))
        ps_o = ctx.enter_context(nc.psum_tensor("ps_o", [P, 2, BANK], F32))

        w_loaded = [sem(f"w_loaded{n}") for n in range(3)]
        x_loaded = [sem(f"x_loaded{g}") for g in range(GROUPS)]
        adj_loaded = [sem(f"adj_loaded{b}") for b in range(ABUFS)]
        res_loaded = [sem(f"res_loaded{b}") for b in range(2)]
        stored = sem("stored")
        ident_zero = sem("ident_zero")
        ident_ready = sem("ident_ready")
        eps_ready = sem("eps_ready")
        w_transposed = sem("w_transposed")
        wq_t_ready = sem("wq_t_ready")
        wk_t_ready = sem("wk_t_ready")
        m_product = sem("m_product")
        m_raw_ready = sem("m_raw_ready")
        w_max_ready = sem("w_max_ready")
        w_gmax_ready = sem("w_gmax_ready")
        w_chain = sem("w_chain")
        w_up_ready = sem("w_up_ready")
        w_hi_ready = sem("w_hi_ready")
        w_lo_ready = sem("w_lo_ready")
        bn_done = sem("bn_done")
        var_ready = sem("var_ready")
        std_ready = sem("std_ready")
        rstd_ready = sem("rstd_ready")
        norm_ready = sem("norm_ready")
        ht_full = sem("ht_full")
        ht_hi_done = sem("ht_hi_done")
        ht_lo_done = sem("ht_lo_done")
        v_full = sem("v_full")
        v_hi_done = sem("v_hi_done")
        v_lo_done = sem("v_lo_done")
        g_full = sem("g_full")
        g_hi_done = sem("g_hi_done")
        g_lo_done = sem("g_lo_done")
        score_full = sem("score_full")
        scaled = sem("scaled")
        bias_ready = sem("bias_ready")
        exp_done = sem("exp_done")
        high_done = sem("high_done")
        low_done = sem("low_done")
        turned = [sem(f"turned{q}") for q in range(PAIRS)]
        weighed = sem("weighed")
        o_chain = sem("o_chain")
        out_ready = sem("out_ready")
        waited_dve = sem("waited_dve")
        waited_sp = sem("waited_sp")

        block = ctx.enter_context(nc.Block())

        def lin(i, per, k):
            return i * per + k

        def main_turns(eng, body):
            with eng.Fori(0, TILES // UNROLL - 1) as i:
                for j in range(UNROLL):
                    body(i, j, False)
            for j in range(UNROLL):
                body(TILES // UNROLL - 1, j, True)

        def there(j, last):
            return not last or j < UNROLL

        @block.sync
        def _(sp):
            sp.dma_start(x_rows[:, 0], x_groups[0]).then_inc(x_loaded[0], 16)
            for n, w in enumerate((w_v, w_q, w_k)):
                sp.dma_start(w_in[:, n, :, :], w.rearrange("(c p) n -> p c n", p=P)).then_inc(w_loaded[n], 16)
            for g in range(1, GROUPS):
                sp.dma_start(x_rows[:, g], x_groups[g]).then_inc(x_loaded[g], 16)
                if g == 3:
                    sp.dma_start(prob[:, 0, :], adj_tiles[0]).then_inc(adj_loaded[0], 16)
            sp.dma_start(prob[:, 1, :], adj_tiles[1]).then_inc(adj_loaded[1], 16)
            for t in range(2):
                sp.dma_start(x_out[:, t, :], x_tiles[t]).then_inc(res_loaded[t], 16)
            for b in (2, 3):
                sp.wait_ge(ht_full, (b - 1) * GROUPS // 2)
                sp.dma_start(prob[:, b, :], adj_tiles[b]).then_inc(adj_loaded[b], 16)

            def await_count(semaphore, count):
                sp.wait_ge(semaphore, count)
                if not isinstance(count, int):
                    sp.sem_inc(waited_sp, 1)

            def transpose_pair(i, j, q):
                await_count(low_done, lin(i, UNROLL * PAIRS, PAIRS * j + q + 1))
                if not (isinstance(i, int) and UNROLL * i + j == 0):
                    await_count(weighed, lin(i, UNROLL * PAIRS, PAIRS * (j - 1) + q + 1))
                sp.dma_start_transpose(parts_t[:, q].rearrange("p h b n -> p (h b) n"),
                                       parts[:, q].rearrange("p h m -> p (h m)")).then_inc(turned[q], 16)

            def load_adj(i, j):
                row = (UNROLL * i + j) * P
                sp.dma_start(prob[:, j % ABUFS, :], adj[bass.ds(row, P), :]).then_inc(adj_loaded[j % ABUFS], 16)

            for q in range(PAIRS):
                transpose_pair(0, 0, q)

            def tile_turn(i, j, last):
                if not last:
                    load_adj(i, j + ABUFS)
                if there(j + 1, last):
                    for q in range(PAIRS):
                        transpose_pair(i, j + 1, q)
                t = UNROLL * i + j
                await_count(out_ready, lin(i, UNROLL, j + 1))
                sp.dma_start(out[bass.ds(t * P, P), :], x_out[:, j % 2, :]).then_inc(stored, 16)
                await_count(stored, lin(i, 16 * UNROLL, 16 * (j + 1)))
                if there(j + 2, last):
                    sp.dma_start(x_out[:, j % 2, :], x[bass.ds((t + 2) * P, P), :]
                                 ).then_inc(res_loaded[j % 2], 16)

            main_turns(sp, tile_turn)

        @block.gpsimd
        def _(pool):
            nc.gpsimd.memset(ln_eps[:], LN_EPS / H_UP ** 2).then_inc(eps_ready, 1)
            nc.gpsimd.memset(ident[:], 0.0).then_inc(ident_zero, 1)
            pool.wait_ge(ident_zero, 1)
            nc.gpsimd.affine_select(out=ident[:], in_=ident[:], compare_op=ALU.not_equal, fill=1.0, base=0,
                                    pattern=[[-1, P]], channel_multiplier=1).then_inc(ident_ready, 1)

            for n in range(2):
                pool.wait_ge(w_max_ready, n + 1)
                nc.gpsimd.partition_all_reduce(w_gmax[:, n:n + 1], w_max[:, n:n + 1], P, ABSMAX
                                               ).then_inc(w_gmax_ready, 1)

        @block.tensor
        def _(pe):
            pe.wait_ge(ident_ready, 1)
            for n in range(2):
                pe.wait_ge(w_loaded[n + 1], 16)
                for k in range(DC):
                    for c in range(DC):
                        last = nc.tensor.transpose(ps_o[:, n, k * D + c * P:k * D + (c + 1) * P],
                                                   w_in[:, n + 1, c, k * P:(k + 1) * P], ident[:])
            last.then_inc(w_transposed, 1)

            def weight_product():
                pe.wait_ge(wq_t_ready, 1)
                pe.wait_ge(wk_t_ready, 1)
                for c in range(DC):
                    for k in range(DC):
                        last = nc.tensor.matmul(ps_s[:, 0, c * D:(c + 1) * D], wq_t[:, k, c * P:(c + 1) * P],
                                                wk_t[:, k, :], start=(k == 0), stop=(k == DC - 1))
                last.then_inc(m_product, 1)

            def transpose_h(g):
                pe.wait_ge(norm_ready, g + 1)
                if g > 0:
                    pe.wait_ge(ht_lo_done, g)
                for d in range(DC):
                    for b in range(BPC):
                        last = nc.tensor.transpose(ps_g[:, d, b * P:(b + 1) * P],
                                                   x_rows[:, g, b, d * P:(d + 1) * P], ident[:])
                last.then_inc(ht_full, 1)

            def project_v(g):
                pe.wait_ge(ht_lo_done, g + 1)
                if g > 0:
                    pe.wait_ge(v_lo_done, g)
                for b in range(BPC):
                    dst = ps_o[:, b // 2, (b % 2) * D:(b % 2 + 1) * D]
                    rows = slice((g * BPC + b) * P, (g * BPC + b + 1) * P)
                    for d in range(DC):
                        for n, (h, w) in enumerate(((ht_hi, wv_hi), (ht_hi, wv_lo), (ht_lo, wv_hi))):
                            last = nc.tensor.matmul(dst, h[:, d, rows], w[:, d, :],
                                                    start=(d == 0 and n == 0), stop=(d == DC - 1 and n == 2))
                last.then_inc(v_full, 1)

            def g_tile(i, j, bank):
                col = (UNROLL * i + j) * P
                for e in range(DC):
                    for d in range(DC):
                        for n, (m, h) in enumerate(((m_hi, ht_hi), (m_hi, ht_lo), (m_lo, ht_hi))):
                            last = nc.tensor.matmul(bank[:, e * P:(e + 1) * P], m[:, d, e * P:(e + 1) * P],
                                                    h[:, d, bass.ds(col, P)],
                                                    start=(d == 0 and n == 0), stop=(d == DC - 1 and n == 2))
                last.then_inc(g_full, 1)

            def score_chunk(i, j, s):
                if s % 2 == 0 and not (isinstance(i, int) and UNROLL * i + j == 0 and s < 4):
                    pe.wait_ge(scaled, lin(i, UNROLL * PAIRS, PAIRS * j + s // 2 - 1))
                if s == 0:
                    pe.wait_ge(g_lo_done, lin(i, UNROLL, j + 1))
                b = j % 2
                dst = ps_s[:, (s // 2) % 2, (s % 2) * BANK:(s % 2 + 1) * BANK]
                cols = slice(s * BANK, (s + 1) * BANK)
                for d in range(DC):
                    for n, (g, h) in enumerate(((g_hi, ht_hi), (g_hi, ht_lo), (g_lo, ht_hi))):
                        last = nc.tensor.matmul(dst, g[:, b, d, :], h[:, d, cols],
                                                start=(d == 0 and n == 0), stop=(d == DC - 1 and n == 2))
                if s % 2 == 1:
                    last.then_inc(score_full, 1)

            def weigh_values(i, j, s):
                q = s // 2
                if s % 2 == 0:
                    pe.wait_ge(turned[q], lin(i, 16 * UNROLL, 16 * (j + 1)))
                for b in range(BPC):
                    m = s * BPC + b
                    col = (s % 2) * BPC + b
                    nc.tensor.matmul(ps_o[:, j % 2, :], parts_t[:, q, 0, col, :], v_hl[:, m, :],
                                     start=(m == 0), stop=False)
                    last = nc.tensor.matmul(ps_o[:, j % 2, 0:D], parts_t[:, q, 1, col, :],
                                            v_hl[:, m, 0:D], start=False, stop=(m == TILES - 1))
                if s % 2 == 1:
                    last.then_inc(weighed, 1)

            transpose_h(0)
            weight_product()
            transpose_h(1)
            pe.wait_ge(w_lo_ready, 1)
            project_v(0)
            pe.wait_ge(w_lo_ready, 2)
            g_tile(0, 0, ps_s[:, 1, :])
            for g in range(GROUPS):
                pe.wait_ge(ht_lo_done, g + 1)
                score_chunk(0, 0, g)
                if g + 2 < GROUPS:
                    transpose_h(g + 2)
                if g + 1 < GROUPS - LATE_V:
                    project_v(g + 1)
            g_tile(0, 1, ps_g[:, 1, :])
            g_tile(0, 2, ps_g[:, 0, :])
            for s in range(LEAD):
                if s % 2 == 0 and s // 2 < LATE_V:
                    project_v(GROUPS - LATE_V + s // 2)
                score_chunk(0, 1, s)
            pe.wait_ge(v_lo_done, GROUPS)

            def tile_turn(i, j, last):
                for r in range(CH):
                    if r < CH - LEAD:
                        if there(j + 1, last):
                            score_chunk(i, j + 1, r + LEAD)
                    elif there(j + 2, last):
                        score_chunk(i, j + 2, r + LEAD - CH)
                    if r == G_STEP and there(j + 3, last):
                        g_tile(i, j + 3, ps_g[:, (j + 3) % 2, :])
                    weigh_values(i, j, r)

            main_turns(pe, tile_turn)

        @block.scalar
        def _(act):
            def std_of(g):
                act.wait_ge(var_ready, g + 1)
                tiles = slice(g * BPC, (g + 1) * BPC)
                nc.scalar.activation(std[:, tiles], mean_var[:, tiles, 1:2], ACT.Sqrt, bias=ln_eps[:, 0:1],
                                     scale=1.0 / H_UP ** 2).then_inc(std_ready, 1)

            def normalise(g):
                act.wait_ge(rstd_ready, 2 * (g + 1))
                for b in range(BPC):
                    t = g * BPC + b
                    last = nc.scalar.activation(x_rows[:, g, b, :], x_rows[:, g, b, :], ACT.Identity,
                                                bias=neg_mean[:, t, :], scale=rstd[:, t, :])
                last.then_inc(norm_ready, 1)

            def high_weights(n, raw, hi):
                act.wait_ge(w_up_ready, n + 1)
                nc.scalar.mul(hi[:], raw, w_up[:, n:n + 1]).then_inc(w_hi_ready, 1)

            def h_high(g):
                act.wait_ge(ht_full, g + 1)
                nc.scalar.activation(ht_hi[:, :, g * BANK:(g + 1) * BANK], ps_g[:, :, :],
                                     ACT.Relu).then_inc(ht_hi_done, 1)

            def v_high(g):
                act.wait_ge(v_full, g + 1)
                nc.scalar.copy(v_hl[:, g * BPC:(g + 1) * BPC, 0:D],
                               ps_o[:, :, :].rearrange("p a (b d) -> p (a b) d", d=D)).then_inc(v_hi_done, 1)

            def g_high(i, j, bank):
                act.wait_ge(g_full, lin(i, UNROLL, j + 1))
                nc.scalar.copy(g_hi[:, j % 2], bank[:, 0:D].rearrange("p (e n) -> p e n", e=DC)
                               ).then_inc(g_hi_done, 1)

            act.wait_ge(eps_ready, 1)
            nc.scalar.activation(table_warm[:, 0:1], ln_eps[:], ACT.Sqrt)
            std_of(0)
            normalise(0)
            act.wait_ge(w_transposed, 1)
            nc.scalar.copy(wq_t[:].rearrange("p a b -> p (a b)"), ps_o[:, 0, :]).then_inc(wq_t_ready, 1)
            std_of(1)
            high_weights(0, w_in[:, 0], wv_hi)
            h_high(0)
            normalise(1)
            act.wait_ge(m_product, 1)
            nc.scalar.copy(m_raw[:].rearrange("p a b -> p (a b)"), ps_s[:, 0, 0:2 * D]).then_inc(m_raw_ready, 1)
            std_of(2)
            h_high(1)
            high_weights(1, m_raw[:], m_hi)
            v_high(0)
            g_high(0, 0, ps_s[:, 1, :])
            normalise(2)
            for g in range(GROUPS):
                if 0 < g < GROUPS - LATE_V:
                    v_high(g)
                if g + 3 < GROUPS:
                    std_of(g + 3)
                if g + 2 < GROUPS:
                    h_high(g + 2)
                if g + 3 < GROUPS:
                    normalise(g + 3)
                if g == GROUPS - 3:
                    nc.scalar.activation(table_warm[:, 1:2], ln_eps[:], ACT.Exp)
            g_high(0, 1, ps_g[:, 1, :])
            g_high(0, 2, ps_g[:, 0, :])

            def bias_of(i, j):
                act.wait_ge(scaled, lin(i, UNROLL * PAIRS, PAIRS * (j + 1)))
                nc.scalar.mul(exp_bias[:, j % 2:j % 2 + 1], p_max[:, j % 2, PAIRS - 1:PAIRS],
                              neg_exp_scale[:, 0:1]).then_inc(bias_ready, 1)
                act.wait_ge(bias_ready, lin(i, UNROLL, j + 1))

            def exp_pair(i, j, q):
                v = prob[:, j % ABUFS, q * PAIR:(q + 1) * PAIR]
                nc.scalar.activation(v, v, ACT.Exp, bias=exp_bias[:, j % 2:j % 2 + 1], scale=exp_scale[:, 0:1],
                                     accum_out=p_sum[:, j % 2, q:q + 1]).then_inc(exp_done, 1)

            def high_parts(i, j, q):
                if not (isinstance(i, int) and UNROLL * i + j == 0):
                    act.wait_ge(turned[q], lin(i, 16 * UNROLL, 16 * j))
                act.wait_ge(exp_done, lin(i, UNROLL * PAIRS, PAIRS * j + q + 1))
                nc.scalar.copy(parts[:, q, 0, :], prob[:, j % ABUFS, q * PAIR:(q + 1) * PAIR]
                               ).then_inc(high_done, 1)

            def exponentials(i, j, between):
                bias_of(i, j)
                for q in range(PAIRS):
                    exp_pair(i, j, q)
                    high_parts(i, j, q)
                    between(q)

            def late_v_high(q):
                if q < LATE_V:
                    v_high(GROUPS - LATE_V + q)

            exponentials(0, 0, late_v_high)

            def tile_turn(i, j, last):
                def g_next(q):
                    if q == 1 and there(j + 3, last):
                        g_high(i, j + 3, ps_g[:, (j + 3) % 2, :])
                if there(j + 1, last):
                    exponentials(i, j + 1, g_next)

            main_turns(act, tile_turn)

        @block.vector
        def _(dve):
            def stats(g):
                dve.wait_ge(x_loaded[g], 16)
                for b in range(BPC):
                    nc.vector.bn_stats(bn[:, g * BPC + b, :], x_rows[:, g, b, :]).then_inc(bn_done, 1)
                for b in range(BPC):
                    t = g * BPC + b
                    dve.wait_ge(bn_done, t + 1)
                    last = nc.vector.bn_aggr(mean_var[:, t, :], bn[:, t, :])
                last.then_inc(var_ready, 1)

            def rstd_of(g):
                dve.wait_ge(std_ready, g + 1)
                tiles = slice(g * BPC, (g + 1) * BPC)
                nc.vector.reciprocal(rstd[:, tiles], std[:, tiles]).then_inc(rstd_ready, 1)
                dve.wait_ge(rstd_ready, 2 * g + 1)
                nc.vector.scalar_tensor_tensor(out=neg_mean[:, tiles], in0=mean_var[:, tiles, 0:1], scalar=-1.0,
                                               in1=rstd[:, tiles], op0=ALU.mult,
                                               op1=ALU.mult).then_inc(rstd_ready, 1)

            def h_low(g):
                dve.wait_ge(ht_hi_done, g + 1)
                cols = slice(g * BANK, (g + 1) * BANK)
                nc.vector.scalar_tensor_tensor(out=ht_lo[:, :, cols], in0=ps_g[:, :, :], scalar=0.0,
                                               in1=ht_hi[:, :, cols], op0=ALU.max,
                                               op1=ALU.subtract).then_inc(ht_lo_done, 1)

            def v_low(g):
                dve.wait_ge(v_hi_done, g + 1)
                tiles = slice(g * BPC, (g + 1) * BPC)
                nc.vector.tensor_tensor(v_hl[:, tiles, D:2 * D],
                                        ps_o[:, :, :].rearrange("p a (b d) -> p (a b) d", d=D),
                                        v_hl[:, tiles, 0:D], ALU.subtract).then_inc(v_lo_done, 1)

            def g_low(i, j, bank):
                dve.wait_ge(g_hi_done, lin(i, UNROLL, j + 1))
                nc.vector.tensor_tensor(g_lo[:, j % 2], bank[:, 0:D].rearrange("p (e n) -> p e n", e=DC),
                                        g_hi[:, j % 2], ALU.subtract).then_inc(g_lo_done, 1)

            def stand_alone():
                dve.sem_inc(waited_dve, 1)

            def scale_pair(i, j, q):
                if q == 0:
                    dve.wait_ge(adj_loaded[j % ABUFS], lin(i, 16, 16 * (j // ABUFS + 1)))
                    start = LOWEST
                else:
                    dve.wait_ge(scaled, lin(i, UNROLL * PAIRS, PAIRS * j + q))
                    start = p_max[:, j % 2, q - 1:q]
                dve.wait_ge(score_full, lin(i, UNROLL * PAIRS, PAIRS * j + q + 1))
                if not isinstance(i, int):
                    stand_alone()
                v = prob[:, j % ABUFS, q * PAIR:(q + 1) * PAIR]
                nc.vector.tensor_tensor_reduce(out=v, in0=ps_s[:, q % 2, :], in1=v, scale=1.0, scalar=start,
                                               op0=ALU.mult, op1=ALU.max,
                                               accum_out=p_max[:, j % 2, q:q + 1]).then_inc(scaled, 1)

            def low_parts(i, j, q):
                dve.wait_ge(high_done, lin(i, UNROLL * PAIRS, PAIRS * j + q + 1))
                nc.vector.tensor_tensor(parts[:, q, 1, :], prob[:, j % ABUFS, q * PAIR:(q + 1) * PAIR],
                                        parts[:, q, 0, :], ALU.subtract).then_inc(low_done, 1)

            def largest(n, raw):
                nc.vector.tensor_reduce(w_max[:, n:n + 1], raw, AX_XY, ALU.max, apply_absolute_value=True
                                        ).then_inc(w_max_ready, 1)

            def weight_scale(n):
                at = slice(n, n + 1)
                dve.wait_ge(w_gmax_ready, n + 1)
                nc.vector.tensor_scalar_max(w_floor[:, at], w_gmax[:, at], TINY).then_inc(w_chain, 1)
                dve.wait_ge(w_chain, 3 * n + 1)
                nc.vector.tensor_scalar(w_pow[:, at].bitcast(U32), w_floor[:, at].bitcast(U32), EXPONENT_BITS,
                                        None, ALU.bitwise_and).then_inc(w_chain, 1)
                dve.wait_ge(w_chain, 3 * n + 2)
                nc.vector.reciprocal(w_inv[:, at], w_pow[:, at]).then_inc(w_chain, 1)
                dve.wait_ge(w_chain, 3 * n + 3)
                nc.vector.tensor_scalar(w_up[:, at], w_inv[:, at], W_TOP / 2, None, ALU.mult
                                        ).then_inc(w_up_ready, 1)

            def low_weights(n, raw, hi, lo):
                dve.wait_ge(w_hi_ready, n + 1)
                nc.vector.scalar_tensor_tensor(out=lo[:], in0=raw, scalar=w_up[:, n:n + 1], in1=hi[:],
                                               op0=ALU.mult, op1=ALU.subtract).then_inc(w_lo_ready, 1)

            stats(0)
            dve.wait_ge(w_loaded[0], 16)
            largest(0, w_in[:, 0])
            rstd_of(0)
            dve.wait_ge(w_transposed, 1)
            nc.vector.tensor_copy(wk_t[:].rearrange("p a b -> p (a b)"), ps_o[:, 1, :]).then_inc(wk_t_ready, 1)
            weight_scale(0)
            nc.vector.tensor_scalar(v_scale[:], w_pow[:, 0:1], 2 / W_TOP / H_UP, None, ALU.mult)
            stats(1)
            rstd_of(1)
            low_weights(0, w_in[:, 0], wv_hi, wv_lo)
            h_low(0)
            stats(2)
            dve.wait_ge(m_raw_ready, 1)
            largest(1, m_raw[:])
            weight_scale(1)
            h_low(1)
            low_weights(1, m_raw[:], m_hi, m_lo)
            exp_unit = 2 / W_TOP / H_UP ** 2 / D ** 0.5
            nc.vector.tensor_scalar(exp_scale[:], w_pow[:, 1:2], exp_unit, None, ALU.mult)
            nc.vector.tensor_scalar(neg_exp_scale[:], w_pow[:, 1:2], -exp_unit, None, ALU.mult)
            rstd_of(2)
            v_low(0)
            g_low(0, 0, ps_s[:, 1, :])
            stats(3)
            for g in range(GROUPS):
                if 0 < g < GROUPS - LATE_V:
                    v_low(g)
                if g + 3 < GROUPS:
                    rstd_of(g + 3)
                if g + 4 < GROUPS:
                    stats(g + 4)
                if g + 2 < GROUPS:
                    h_low(g + 2)
                if g % 2 == 1:
                    scale_pair(0, 0, g // 2)
            g_low(0, 1, ps_g[:, 1, :])
            g_low(0, 2, ps_g[:, 0, :])

            def result(i, j):
                b = j % 2
                dve.wait_ge(exp_done, lin(i, UNROLL * PAIRS, PAIRS * (j + 1)))
                nc.vector.reduce_sum(p_tot[:, b:b + 1], p_sum[:, b, :], AX_X).then_inc(o_chain, 1)
                dve.wait_ge(o_chain, lin(i, 4 * UNROLL, 4 * j + 1))
                nc.vector.reciprocal(p_inv[:, b:b + 1], p_tot[:, b:b + 1]).then_inc(o_chain, 1)
                dve.wait_ge(o_chain, lin(i, 4 * UNROLL, 4 * j + 2))
                nc.vector.tensor_tensor(o_scale[:, b:b + 1], p_inv[:, b:b + 1], v_scale[:],
                                        ALU.mult).then_inc(o_chain, 1)
                dve.wait_ge(o_chain, lin(i, 4 * UNROLL, 4 * j + 3))
                dve.wait_ge(weighed, lin(i, UNROLL * PAIRS, PAIRS * (j + 1)))
                dve.wait_ge(res_loaded[b], lin(i, 16 * UNROLL // 2, 16 * (j // 2 + 1)))
                nc.vector.scalar_tensor_tensor(out=x_out[:, b, :], in0=ps_o[:, b, D:2 * D],
                                               scalar=o_scale[:, b:b + 1], in1=x_out[:, b, :], op0=ALU.mult,
                                               op1=ALU.add).then_inc(o_chain, 1)
                dve.wait_ge(o_chain, lin(i, 4 * UNROLL, 4 * j + 4))
                nc.vector.scalar_tensor_tensor(out=x_out[:, b, :], in0=ps_o[:, b, 0:D],
                                               scalar=o_scale[:, b:b + 1], in1=x_out[:, b, :], op0=ALU.mult,
                                               op1=ALU.add).then_inc(out_ready, 1)

            assert LATE_V == 2
            low_parts(0, 0, 0)
            v_low(GROUPS - 2)
            scale_pair(0, 1, 0)
            low_parts(0, 0, 1)
            v_low(GROUPS - 1)
            scale_pair(0, 1, 1)
            low_parts(0, 0, 2)
            low_parts(0, 0, 3)
            scale_pair(0, 1, 2)

            def tile_turn(i, j, last):
                if there(j + 1, last):
                    scale_pair(i, j + 1, 3)
                    low_parts(i, j + 1, 0)
                    if there(j + 2, last):
                        scale_pair(i, j + 2, 0)
                    low_parts(i, j + 1, 1)
                    if there(j + 3, last):
                        g_low(i, j + 3, ps_g[:, (j + 3) % 2, :])
                    low_parts(i, j + 1, 2)
                    low_parts(i, j + 1, 3)
                    if there(j + 2, last):
                        scale_pair(i, j + 2, 1)
                        scale_pair(i, j + 2, 2)
                result(i, j)

            main_turns(dve, tile_turn)


_INS = ["x", "adj", "L0_gnn_W_Q", "L0_gnn_W_K", "L0_gnn_W_V"]
_OUTS = [((4096, 256), "float32")]


def kernel(**inputs):
    import numpy as _np
    import concourse.bacc as _bacc
    from concourse import mybir as _mybir
    from concourse.bass_utils import run_bass_kernel_spmd as _run

    nc = _bacc.Bacc("TRN2", target_bir_lowering=False, num_devices=1)
    arrays, args = {}, []
    for name in _INS:
        a = _np.ascontiguousarray(inputs[name])
        arrays[f"in_{name}_dram"] = a
        args.append(nc.dram_tensor(f"in_{name}_dram", a.shape, _mybir.dt.from_np(a.dtype), kind="ExternalInput").ap())
    for i, (shape, dtype) in enumerate(_OUTS):
        dt = _mybir.dt.from_np(_np.dtype(dtype))
        args.append(nc.dram_tensor(f"out_{i}_dram", shape, dt, kind="ExternalOutput").ap())
    gnn_layer(nc, *args)
    r = _run(nc, [arrays], core_ids=[0])
    got = tuple(r.results[0][f"out_{i}_dram"] for i in range(len(_OUTS)))
    return got[0]
```
